# Optimizing a Trainium2 kernel written in Bass

```python
import numpy as np
import jax
import jax.numpy as jnp

def _softmax(x, axis=-1):
    return jax.nn.softmax(x, axis=axis)

def _gelu(x):
    return jax.nn.gelu(x, approximate=True)

def _silu(x):
    return jax.nn.silu(x)

def _sigmoid(x):
    return jax.nn.sigmoid(x)

def _layernorm(x, axis=-1, eps=1e-05):
    m = jnp.mean(x, axis=axis, keepdims=True)
    v = jnp.var(x, axis=axis, keepdims=True)
    return (x - m) / jnp.sqrt(v + eps)

def _scatter_add(tgt, idx, src, axis=0):
    return tgt.at[idx].add(src)

def _segment_sum(src, seg, n):
    return jax.ops.segment_sum(src, seg, n)
kernel_name = 'mk_gnn_preln_d4_gnn_r32_43fb24'

def setup_inputs(seed: int=0):
    np.random.seed(seed)
    _w = jnp.asarray

    def _rec_inputs():
        import jax
        import jax.numpy as jnp
        _gk = jax.random.key(seed)
        x = -0.000202 + 1 * jax.random.normal(jax.random.fold_in(_gk, 1), (50000, 64), jnp.float32)
        src = jax.random.randint(jax.random.fold_in(_gk, 2), (50000,), 0, 50000, jnp.int32)
        dst = jnp.minimum((50000 * jax.random.uniform(jax.random.fold_in(_gk, 3), (50000,)) ** 2.0).astype(jnp.int32), 49999)
        _o = jnp.argsort(dst, stable=True)
        src = src[_o]
        dst = dst[_o]
        edge_attr_64 = -8.16379e-05 + 0.999858 * jax.random.normal(jax.random.fold_in(_gk, 12), (50000, 64), jnp.float32)
        edge_type_16 = jax.random.randint(jax.random.fold_in(_gk, 14), (50000,), 0, 16, jnp.int32)
        edge_type_8 = jax.random.randint(jax.random.fold_in(_gk, 15), (50000,), 0, 8, jnp.int32)
        edge_weight = jax.random.uniform(jax.random.fold_in(_gk, 16), (50000,), jnp.float32, 0.0, 1)
        return (x, src, dst, edge_attr_64, edge_type_16, edge_type_8, edge_weight)
    x, src, dst, edge_attr_64, edge_type_16, edge_type_8, edge_weight = _rec_inputs()

    def _L0_gnn_setup():
        import jax, jax.numpy as jnp
        import numpy as np
        N_NODES = 3125

        def gcn_conv(x, edge_index, W, b, num_nodes):
            src = jnp.concatenate([edge_index[0], jnp.arange(num_nodes, dtype=edge_index.dtype)])
            dst = jnp.concatenate([edge_index[1], jnp.arange(num_nodes, dtype=edge_index.dtype)])
            deg = jax.ops.segment_sum(jnp.ones_like(dst, dtype=x.dtype), dst, num_segments=num_nodes)
            dinv = jnp.where(deg > 0, jax.lax.rsqrt(deg), 0.0)
            norm = dinv[src] * dinv[dst]
            h = x @ W
            msg = h[src] * norm[:, None]
            out = jax.ops.segment_sum(msg, dst, num_segments=num_nodes)
            return out + b
        key = jax.random.key(seed)
        k1, k2, k3, k4, k5, k6 = jax.random.split(key, 6)
        d_in, d_hid, d_out = (64, 64, 64)
        x = jax.random.normal(k1, (N_NODES, d_in), dtype=jnp.float32)
        edge_index = jax.random.randint(k2, (2, 31250), 0, N_NODES, dtype=jnp.int64)
        W1 = jax.random.normal(k3, (d_in, d_hid), dtype=jnp.float32) / np.sqrt(d_in)
        b1 = jnp.zeros((d_hid,), dtype=jnp.float32)
        W2 = jax.random.normal(k4, (d_hid, d_out), dtype=jnp.float32) / np.sqrt(d_hid)
        b2 = jnp.zeros((d_out,), dtype=jnp.float32)
        return {'x': x, 'edge_index': edge_index, 'W1': W1, 'b1': b1, 'W2': W2, 'b2': b2}
    _L0_gnn_all = _L0_gnn_setup()
    _L0_gnn_in = {k: v for k, v in _L0_gnn_all.items() if k in ('W1', 'b1', 'W2', 'b2')}
    del _L0_gnn_all

    def _L1_gnn_setup():
        import jax, jax.numpy as jnp
        import numpy as np
        N_NODES = 50000
        N_EDGES = 25000
        D_IN = 64
        D_OUT = 64
        NUM_RELS = 16
        key = jax.random.key(seed)
        k1, k2, k3, k4, k5 = jax.random.split(key, 5)
        feat = jax.random.normal(k1, (N_NODES, D_IN), dtype=jnp.float32)
        weight = jax.random.normal(k2, (NUM_RELS, D_IN, D_OUT), dtype=jnp.float32) * 0.05
        src = jax.random.randint(k3, (N_EDGES,), 0, N_NODES, dtype=jnp.int32)
        dst = jax.random.randint(k4, (N_EDGES,), 0, N_NODES, dtype=jnp.int32)
        etypes = jax.random.randint(k5, (N_EDGES,), 0, NUM_RELS, dtype=jnp.int32)
        return {'feat': feat, 'weight': weight, 'src': src, 'dst': dst, 'etypes': etypes}
    _L1_gnn_all = _L1_gnn_setup()
    _L1_gnn_in = {k: v for k, v in _L1_gnn_all.items() if k in ('weight',)}
    del _L1_gnn_all

    def _L2_gnn_setup():
        import jax, jax.numpy as jnp
        import numpy as np
        BN_EPS = 1e-05

        def _batchnorm(x, gamma, beta):
            m = jnp.mean(x, axis=0)
            v = jnp.var(x, axis=0)
            return (x - m) * jax.lax.rsqrt(v + BN_EPS) * gamma + beta
        N, E, D = (3125, 50000, 64)
        key = jax.random.key(seed)
        ks = jax.random.split(key, 6)
        return {'node_feats': jax.random.normal(ks[0], (N, D), dtype=jnp.float32), 'edge_feats': jax.random.normal(ks[1], (E, D), dtype=jnp.float32), 'src': jax.random.randint(ks[2], (E,), 0, N, dtype=jnp.int32), 'dst': jax.random.randint(ks[3], (E,), 0, N, dtype=jnp.int32), 'eps': jnp.zeros((1,), dtype=jnp.float32), 'W1': jax.random.normal(ks[4], (D, 2 * D), dtype=jnp.float32) * (1.0 / np.sqrt(D)), 'b1': jnp.zeros((2 * D,), dtype=jnp.float32), 'gamma1': jnp.ones((2 * D,), dtype=jnp.float32), 'beta1': jnp.zeros((2 * D,), dtype=jnp.float32), 'W2': jax.random.normal(ks[5], (2 * D, D), dtype=jnp.float32) * (1.0 / np.sqrt(2 * D)), 'b2': jnp.zeros((D,), dtype=jnp.float32), 'gamma2': jnp.ones((D,), dtype=jnp.float32), 'beta2': jnp.zeros((D,), dtype=jnp.float32)}
    _L2_gnn_all = _L2_gnn_setup()
    _L2_gnn_in = {k: v for k, v in _L2_gnn_all.items() if k in ('eps', 'W1', 'b1', 'gamma1', 'beta1', 'W2', 'b2', 'gamma2', 'beta2')}
    del _L2_gnn_all

    def _L3_gnn_setup():
        import jax, jax.numpy as jnp
        import numpy as np
        N_NODES = 50000
        N_EDGES = 31250
        D_IN = 64
        D_OUT = 64
        N_REL = 8
        key = jax.random.key(seed)
        ks = jax.random.split(key, 8)
        x = jax.random.normal(ks[0], (N_NODES, D_IN), dtype=jnp.float32)
        edge_src = jax.random.randint(ks[1], (N_EDGES,), 0, N_NODES, dtype=jnp.int32)
        edge_dst = jax.random.randint(ks[2], (N_EDGES,), 0, N_NODES, dtype=jnp.int32)
        edge_rel = jax.random.randint(ks[3], (N_EDGES,), 0, N_REL, dtype=jnp.int32)
        edge_weight = jnp.ones((N_EDGES,), dtype=jnp.float32)
        W_linear = jax.random.normal(ks[4], (N_REL * D_IN, D_OUT), dtype=jnp.float32) * (1.0 / np.sqrt(N_REL * D_IN))
        b_linear = jnp.zeros((D_OUT,), dtype=jnp.float32)
        W_self = jax.random.normal(ks[5], (D_IN, D_OUT), dtype=jnp.float32) * (1.0 / np.sqrt(D_IN))
        b_self = jnp.zeros((D_OUT,), dtype=jnp.float32)
        return {'x': x, 'edge_src': edge_src, 'edge_dst': edge_dst, 'edge_rel': edge_rel, 'edge_weight': edge_weight, 'W_linear': W_linear, 'b_linear': b_linear, 'W_self': W_self, 'b_self': b_self}
    _L3_gnn_all = _L3_gnn_setup()
    _L3_gnn_in = {k: v for k, v in _L3_gnn_all.items() if k in ('W_linear', 'b_linear', 'W_self', 'b_self')}
    del _L3_gnn_all
    return {'x': x, 'src': src, 'dst': dst, 'edge_attr_64': edge_attr_64, 'edge_type_16': edge_type_16, 'edge_type_8': edge_type_8, 'edge_weight': edge_weight, 'L0_gnn_W1': _L0_gnn_in['W1'], 'L0_gnn_b1': _L0_gnn_in['b1'], 'L0_gnn_W2': _L0_gnn_in['W2'], 'L0_gnn_b2': _L0_gnn_in['b2'], 'L1_gnn_weight': _L1_gnn_in['weight'], 'L2_gnn_eps': _L2_gnn_in['eps'], 'L2_gnn_W1': _L2_gnn_in['W1'], 'L2_gnn_b1': _L2_gnn_in['b1'], 'L2_gnn_gamma1': _L2_gnn_in['gamma1'], 'L2_gnn_beta1': _L2_gnn_in['beta1'], 'L2_gnn_W2': _L2_gnn_in['W2'], 'L2_gnn_b2': _L2_gnn_in['b2'], 'L2_gnn_gamma2': _L2_gnn_in['gamma2'], 'L2_gnn_beta2': _L2_gnn_in['beta2'], 'L3_gnn_W_linear': _L3_gnn_in['W_linear'], 'L3_gnn_b_linear': _L3_gnn_in['b_linear'], 'L3_gnn_W_self': _L3_gnn_in['W_self'], 'L3_gnn_b_self': _L3_gnn_in['b_self']}

def reference(x, src, dst, edge_attr_64, edge_type_16, edge_type_8, edge_weight, L0_gnn_W1, L0_gnn_b1, L0_gnn_W2, L0_gnn_b2, L1_gnn_weight, L2_gnn_eps, L2_gnn_W1, L2_gnn_b1, L2_gnn_gamma1, L2_gnn_beta1, L2_gnn_W2, L2_gnn_b2, L2_gnn_gamma2, L2_gnn_beta2, L3_gnn_W_linear, L3_gnn_b_linear, L3_gnn_W_self, L3_gnn_b_self):
    import jax
    import jax.numpy as jnp

    def _L0_gnn_ref(x, edge_index, W1, b1, W2, b2):
        import jax, jax.numpy as jnp
        import numpy as np
        N_NODES = 3125

        def gcn_conv(x, edge_index, W, b, num_nodes):
            src = jnp.concatenate([edge_index[0], jnp.arange(num_nodes, dtype=edge_index.dtype)])
            dst = jnp.concatenate([edge_index[1], jnp.arange(num_nodes, dtype=edge_index.dtype)])
            deg = jax.ops.segment_sum(jnp.ones_like(dst, dtype=x.dtype), dst, num_segments=num_nodes)
            dinv = jnp.where(deg > 0, jax.lax.rsqrt(deg), 0.0)
            norm = dinv[src] * dinv[dst]
            h = x @ W
            msg = h[src] * norm[:, None]
            out = jax.ops.segment_sum(msg, dst, num_segments=num_nodes)
            return out + b
        n = x.shape[0]
        h = jax.nn.relu(gcn_conv(x, edge_index, W1, b1, n))
        out = jax.nn.relu(gcn_conv(h, edge_index, W2, b2, n))
        return out

    def _L1_gnn_ref(feat, weight, src, dst, etypes):
        import jax, jax.numpy as jnp
        import numpy as np
        N_NODES = 50000
        N_EDGES = 25000
        D_IN = 64
        D_OUT = 64
        NUM_RELS = 16
        num_rels = weight.shape[0]
        h_src = feat[src]
        msg = jnp.zeros((h_src.shape[0], weight.shape[2]), dtype=feat.dtype)
        for r in range(num_rels):
            mask = etypes == r
            msg = msg + h_src * mask[:, None].astype(feat.dtype) @ weight[r]
        out = jax.ops.segment_sum(msg, dst, num_segments=feat.shape[0])
        return out

    def _L2_gnn_ref(node_feats, edge_feats, src, dst, eps, W1, b1, gamma1, beta1, W2, b2, gamma2, beta2):
        import jax, jax.numpy as jnp
        import numpy as np
        BN_EPS = 1e-05

        def _batchnorm(x, gamma, beta):
            m = jnp.mean(x, axis=0)
            v = jnp.var(x, axis=0)
            return (x - m) * jax.lax.rsqrt(v + BN_EPS) * gamma + beta
        N = node_feats.shape[0]
        msg = node_feats[src] + edge_feats
        agg_sum = jax.ops.segment_sum(msg, dst, num_segments=N)
        deg = jax.ops.segment_sum(jnp.ones((src.shape[0],), dtype=node_feats.dtype), dst, num_segments=N)
        agg_mean = agg_sum / jnp.maximum(deg, 1.0)[:, None]
        h = (1.0 + eps[0]) * node_feats + agg_mean
        h = jax.nn.relu(_batchnorm(h @ W1 + b1, gamma1, beta1))
        h = jax.nn.relu(_batchnorm(h @ W2 + b2, gamma2, beta2))
        return h

    def _L3_gnn_ref(x, edge_src, edge_dst, edge_rel, edge_weight, W_linear, b_linear, W_self, b_self):
        import jax, jax.numpy as jnp
        import numpy as np
        N_NODES = 50000
        N_EDGES = 31250
        D_IN = 64
        D_OUT = 64
        N_REL = 8
        N, d = x.shape
        R = W_linear.shape[0] // d
        seg = edge_dst * R + edge_rel
        deg = jax.ops.segment_sum(edge_weight, seg, num_segments=N * R)
        ew = edge_weight / deg[seg]
        msg = x[edge_src] * ew[:, None]
        update = jax.ops.segment_sum(msg, seg, num_segments=N * R)
        update = update.reshape(N, R * d)
        out = update @ W_linear + b_linear + x @ W_self + b_self
        return jax.nn.relu(out)
    edge_index = jnp.stack([src, dst])
    h = jnp.maximum(_layernorm(x, axis=-1), 0.0)
    x = x + _L0_gnn_ref(h, edge_index, L0_gnn_W1, L0_gnn_b1, L0_gnn_W2, L0_gnn_b2)
    h = jnp.maximum(_layernorm(x, axis=-1), 0.0)
    x = x + _L1_gnn_ref(h, L1_gnn_weight, src, dst, edge_type_16)
    h = jnp.maximum(_layernorm(x, axis=-1), 0.0)
    x = x + _L2_gnn_ref(h, edge_attr_64, src, dst, L2_gnn_eps, L2_gnn_W1, L2_gnn_b1, L2_gnn_gamma1, L2_gnn_beta1, L2_gnn_W2, L2_gnn_b2, L2_gnn_gamma2, L2_gnn_beta2)
    h = jnp.maximum(_layernorm(x, axis=-1), 0.0)
    x = x + _L3_gnn_ref(h, src, dst, edge_type_8, edge_weight, L3_gnn_W_linear, L3_gnn_b_linear, L3_gnn_W_self, L3_gnn_b_self)
    return x

_drawn_inputs = setup_inputs


def setup_inputs(seed=0):
    import zlib

    import numpy as np

    out = dict(_drawn_inputs(seed))
    spreads = {'L0_gnn_b1': (0.0, 0.1),
     'L0_gnn_b2': (0.0, 0.1),
     'L2_gnn_b1': (0.0, 0.1),
     'L2_gnn_gamma1': (1.0, 0.2),
     'L2_gnn_beta1': (0.0, 0.1),
     'L2_gnn_b2': (0.0, 0.1),
     'L2_gnn_gamma2': (1.0, 0.2),
     'L2_gnn_beta2': (0.0, 0.1),
     'L3_gnn_b_linear': (0.0, 0.1),
     'L3_gnn_b_self': (0.0, 0.1)}
    factors = {}
    for name, (base, spread) in spreads.items():
        noise = np.random.default_rng([zlib.crc32(name.encode()), seed]).standard_normal(out[name].shape)
        drawn = base * np.exp(spread * noise) if base else spread * noise
        out[name] = jnp.asarray(drawn.astype(out[name].dtype))
    for name, factor in factors.items():
        out[name] = (out[name] * factor).astype(out[name].dtype)
    return out
```

```python
from contextlib import ExitStack

import concourse.bass as bass
from concourse import mybir

F32 = mybir.dt.float32
F16 = mybir.dt.float16
I32 = mybir.dt.int32
ALU = mybir.AluOpType
ACT = mybir.ActivationFunctionType
AX = mybir.AxisListType

P = 128
N = 50000
E = 50000
D = 64
T = 392
ROWS = P * T
LAST = N - (P - 1) * T
TRASH = ROWS
AGG_ROWS = ROWS + P
B = 7
HALVES = T // B
GN = 4
GROUPS = T // GN
FULL = LAST // GN
COLS = GN * P
R16, R8 = 16, 8
W0 = 2 * D + R8
EPS = 1e-5
ROUND = 12582912.0
ZCH = 3144


def at(h, per, k):
    if isinstance(h, int):
        return h * per + k
    r, s = h
    return r * (2 * per) + (s * per + k)


def half_of(h, lag):
    if isinstance(h, int):
        return h - lag
    r, s = h
    return (r, s - lag)


def pairs(eng, first, end, body, tail=0, peel=None):
    peeled = first + (peel or (4 if tail else 2))
    for h in range(first, peeled):
        body(h, h % 2)
    with eng.Fori(peeled // 2, end // 2, 1) as r:
        for s in range(2):
            body((r, s), s)
    for h in range(end, end + tail):
        body(h, h % 2)


def reached(eng, semaphore, value):
    eng.wait_ge(semaphore, value)
    if not isinstance(value, int):
        eng.sem_inc(PASSED[0], 1)


PASSED = [None]


def static(h):
    return isinstance(h, int)


def build(nc, x, src, dst, edge_attr, type16, type8, weight, l0_w1, l0_b1, l0_w2, l0_b2, l1_w,
          l2_eps, l2_w1, l2_b1, l2_gamma1, l2_beta1, l2_w2, l2_b2, l2_gamma2, l2_beta2,
          l3_wl, l3_bl, l3_ws, l3_bs, out):
    ctx = ExitStack()
    with ctx:
        def sb(name, shape, dt=F32):
            return ctx.enter_context(nc.sbuf_tensor(name, shape, dt))

        PASSED[0] = ctx.enter_context(nc.semaphore("passed"))
        phase_sems = []

        def sem(name):
            phase_sems.append(nc.alloc_semaphore(name=name))
            return phase_sems[-1]

        def phase(build_phase, *a):
            phase_sems.clear()
            build_phase(*a)
            nc.clear_and_free_semaphores(phase_sems)
            nc.all_engine_barrier()

        def dram(name, shape):
            return nc.dram_tensor(name, shape, F32, kind="Internal").ap()

        table = [dram(f"table{k}", [ROWS, D]) for k in range(5)]
        widths = [W0, D, D, D, D]
        agg = [[dram(f"agg{k}_{q}", [AGG_ROWS, widths[k]]) for q in range(2)] for k in range(5)]
        rel_deg = dram("rel_deg", [AGG_ROWS, R8])
        g_dram = dram("g_dram", [D, GROUPS * COLS])
        y_dram = dram("y_dram", [D, GROUPS * COLS])

        xr = sb("xr", [P, T, D])
        src_i = sb("src_i", [P, T], I32)
        dst_i = sb("dst_i", [P, T], I32)
        out_i = sb("out_i", [P, T], I32)
        dst_f = sb("dst_f", [P, T])
        t16_f = sb("t16_f", [P, T])
        t8_f = sb("t8_f", [P, T])
        w_f = sb("w_f", [P, T])
        dinv = sb("dinv", [P, T])
        rdeg = sb("rdeg", [P, T])
        edge_rel = sb("edge_rel", [P, T, R8])
        ident = sb("ident", [P, P])
        lower = sb("lower", [P, P])
        iota16 = sb("iota16", [P, R16])
        iota_i = sb("iota_i", [P, T], I32)
        iota_h = sb("iota_h", [P, T], F16)
        part_i = sb("part_i", [P, 1], I32)
        trash_f = sb("trash_f", [P, 1])
        zeros = sb("zeros", [P, ZCH])
        w01 = sb("w01", [D + 1, D])
        w02 = sb("w02", [D + 1, D])
        w1t = sb("w1t", [P, R16 // 2, D])
        w21 = sb("w21", [D + 1, 2 * D])
        w22 = sb("w22", [P, D])
        w3t = sb("w3t", [P, R8 // 2, D])
        w3s = sb("w3s", [D + 2, D])
        eps1 = sb("eps1", [P, 1])
        gb1 = sb("gb1", [P, 2])
        gb2 = sb("gb2", [D, 3])
        nrm1 = sb("nrm1", [P, 8])
        nrm2 = sb("nrm2", [D, 8])

        big = sb("big", [P, 10240])
        ixs = sb("ixs", [P, 2, B], I32)
        ixo = sb("ixo", [P, 2, B], I32)
        row_stats = sb("row_stats", [P, T, 6])
        mean = sb("mean", [P, T])
        rstd = sb("rstd", [P, T])
        bnst = sb("bnst", [P, GROUPS, 6])
        ps = ctx.enter_context(nc.psum_tensor("ps", [P, 8, 512], F32))

        cut_at = [0]

        def cut(shape):
            n = 1
            for d in shape:
                n *= d
            a = big[:, cut_at[0]:cut_at[0] + n]
            cut_at[0] += n
            assert cut_at[0] <= 10240, cut_at
            if len(shape) == 1:
                return a
            names = " ".join(f"d{i}" for i in range(len(shape)))
            return a.rearrange(f"p ({names}) -> p {names}", **{f"d{i}": d for i, d in enumerate(shape)})

        def node_view(t):
            return t.rearrange("(p t) f -> p t f", t=T)

        def zero_aggregate(eng, k, zeroed):
            for q in range(2):
                flat = agg[k][q].rearrange("(p r) f -> p (r f)", p=P)
                n = flat.shape[1] // ZCH
                eng.dma_start(flat.rearrange("p (c z) -> p c z", c=n),
                              zeros[:, :].unsqueeze(1).to_broadcast([P, n, ZCH])).then_inc(zeroed, 16)

        def phase_plan():
            cut_at[0] = 0
            tmp = cut([T])
            node_p = cut([T])
            node_t = cut([T])
            raw = [cut([T]).bitcast(I32) for _ in range(2)]
            hot_p = cut([2 * B * P // 2]).bitcast(F16).rearrange("p (s b c) -> p s b c", s=2, b=B)
            hot_t = cut([2 * B * T // 2]).bitcast(F16).rearrange("p (s b c) -> p s b c", s=2, b=B)
            loads, filled, consts, cast = sem("plan_loads"), sem("plan_filled"), sem("plan_consts"), sem("plan_cast")
            hot_ready, hot_used, deg_ready, deg_dve = sem("hot_ready"), sem("hot_used"), sem("deg_ready"), sem("deg_dve")
            root, zeroed = sem("root"), sem("zeroed")
            n_loads = [0]
            with nc.Block() as block:
                @block.gpsimd
                def _(pool):
                    pads = slice(LAST, T)
                    nc.gpsimd.memset(dst_i[96:P, pads], ROWS + P - 1).then_inc(filled, 1)
                    nc.gpsimd.memset(src_i[96:P, pads], 0).then_inc(filled, 1)
                    for r in raw:
                        nc.gpsimd.memset(r[96:P, pads], 0).then_inc(filled, 1)
                    nc.gpsimd.memset(w_f[96:P, pads], 0.0).then_inc(filled, 1)
                    nc.gpsimd.memset(xr[96:P, pads, :], 0.0).then_inc(filled, 1)
                    pool.wait_ge(filled, 6)
                    nc.gpsimd.iota(iota_i[:, :], pattern=[[1, T]], base=0, channel_multiplier=0).then_inc(consts, 1)
                    nc.gpsimd.iota(part_i[:, :], pattern=[[0, 1]], base=TRASH, channel_multiplier=1).then_inc(consts, 1)
                    nc.gpsimd.memset(zeros[:, :], 0.0).then_inc(consts, 1)
                    nc.gpsimd.memset(ident[:, :], 0.0).then_inc(consts, 1)
                    nc.gpsimd.memset(lower[:, :], 1.0).then_inc(consts, 1)
                    reached(pool, consts, 5)
                    nc.gpsimd.affine_select(out=ident[:, :], in_=ident[:, :], compare_op=ALU.not_equal, fill=1.0,
                                            base=0, pattern=[[-1, P]], channel_multiplier=1).then_inc(consts, 1)
                    nc.gpsimd.affine_select(out=lower[:, :], in_=lower[:, :], compare_op=ALU.is_gt, fill=0.0,
                                            base=0, pattern=[[-1, P]], channel_multiplier=1).then_inc(consts, 1)

                @block.sync
                def _(sp):
                    def load(to, of):
                        n_loads[0] += 1
                        sp.dma_start(to, of).then_inc(loads, 16)

                    reached(sp, filled, 6)
                    for to, of in ((dst_i, dst), (src_i, src), (raw[0], type16), (raw[1], type8), (w_f, weight)):
                        load(to[0:P - 1, :], of[0:(P - 1) * T].rearrange("(p t) -> p t", t=T))
                        load(to[P - 1:P, 0:LAST], of[(P - 1) * T:E].rearrange("(p t) -> p t", p=1))
                    load(w01[0:D, :], l0_w1)
                    load(w01[D:D + 1, :], l0_b1.rearrange("(a f) -> a f", a=1))
                    load(w02[0:D, :], l0_w2)
                    load(w02[D:D + 1, :], l0_b2.rearrange("(a f) -> a f", a=1))
                    load(w1t[:, :, :], l1_w.rearrange("(q c) k f -> (c k) q f", c=2))
                    load(w21[0:D, :], l2_w1)
                    load(w21[D:D + 1, :], l2_b1.rearrange("(a f) -> a f", a=1))
                    load(w22[:, :], l2_w2)
                    load(w3t[:, :, :], l3_wl.rearrange("(q p) f -> p q f", p=P))
                    load(w3s[0:D, :], l3_ws)
                    load(w3s[D:D + 1, :], l3_bl.rearrange("(a f) -> a f", a=1))
                    load(w3s[D + 1:D + 2, :], l3_bs.rearrange("(a f) -> a f", a=1))
                    load(eps1[:, :], l2_eps.rearrange("(a b) -> a b", a=1).to_broadcast([P, 1]))
                    for c, v in enumerate((l2_gamma1, l2_beta1)):
                        load(gb1[:, c:c + 1], v.rearrange("(p a) -> p a", a=1))
                    for c, v in enumerate((l2_gamma2, l2_beta2, l2_b2)):
                        load(gb2[:, c:c + 1], v.rearrange("(p a) -> p a", a=1))
                    xv = x[0:(P - 1) * T, :].rearrange("(p t) f -> p t f", t=T)
                    load(xr[0:112, :, :], xv[0:112, :, :])
                    load(xr[112:P - 1, :, :], xv[112:P - 1, :, :])
                    load(xr[P - 1:P, 0:LAST, :], x[(P - 1) * T:N, :].rearrange("(p t) f -> p t f", p=1))
                    reached(sp, consts, 5)
                    zero_aggregate(sp, 0, zeroed)
                    reached(sp, deg_dve, 5)
                    sp.dma_start(rel_deg[ROWS:AGG_ROWS, :], tmp[:, 0:R8]).then_inc(loads, 16)
                    reached(sp, loads, 16 * (n_loads[0] + 1))
                    reached(sp, zeroed, 32)

                @block.vector
                def _(dve):
                    nc.vector.memset(tmp[:, :], 1.0)
                    dve.wait_ge(consts, 3)
                    nc.vector.tensor_copy(iota_h[:, :], iota_i[:, :]).then_inc(cast, 1)
                    nc.vector.tensor_copy(iota16[:, :], iota_i[:, 0:R16]).then_inc(cast, 1)
                    nc.vector.tensor_copy(trash_f[:, :], part_i[:, :]).then_inc(cast, 1)
                    dve.wait_ge(loads, 16 * n_loads[0])
                    nc.vector.tensor_copy(dst_f[:, :], dst_i[:, :]).then_inc(cast, 1)
                    nc.vector.tensor_copy(t16_f[:, :], raw[0]).then_inc(cast, 1)
                    nc.vector.tensor_copy(t8_f[:, :], raw[1]).then_inc(cast, 1)
                    dve.wait_ge(cast, 6)
                    nc.vector.tensor_scalar(node_t[:, :], dst_f[:, :], 0.5, 1.0 / T, ALU.add, ALU.mult).then_inc(cast, 1)
                    dve.wait_ge(cast, 7)
                    nc.vector.tensor_scalar(node_t[:, :], node_t[:, :], -0.5, ROUND, ALU.add, ALU.add).then_inc(cast, 1)
                    dve.wait_ge(cast, 8)
                    nc.vector.tensor_scalar(node_p[:, :], node_t[:, :], -ROUND, None, ALU.add).then_inc(cast, 1)
                    dve.wait_ge(cast, 9)
                    nc.vector.scalar_tensor_tensor(node_t[:, :], node_p[:, :], float(-T), dst_f[:, :],
                                                   ALU.mult, ALU.add).then_inc(cast, 1)
                    dve.wait_ge(cast, 10)

                    def hots(h, s):
                        if not (static(h) and h < 2):
                            dve.wait_ge(hot_used, at(h, 1, -1))
                        for b in range(B):
                            col = bass.ds(at(h, B, b), 1)
                            nc.vector.tensor_scalar(hot_p[:, s, b, :], iota_h[:, 0:P], node_p[:, col], None, ALU.is_equal)
                            last = nc.vector.tensor_scalar(hot_t[:, s, b, :], iota_h[:, :], node_t[:, col], None, ALU.is_equal)
                        last.then_inc(hot_ready, 1)

                    pairs(dve, 0, HALVES, hots)
                    pairs(dve, 0, GROUPS, lambda h, s: layer_stats(h))
                    dve.wait_ge(deg_ready, 1)
                    nc.vector.tensor_scalar(dinv[:, :], ps[:, 0, 0:T], 1.0, None, ALU.add).then_inc(deg_dve, 1)
                    nc.vector.tensor_scalar(rdeg[:, :], ps[:, 0, 0:T], 1.0, None, ALU.max).then_inc(deg_dve, 1)
                    dve.wait_ge(deg_dve, 2)
                    dve.wait_ge(root, 1)
                    nc.vector.reciprocal(dinv[:, :], node_p[:, :]).then_inc(deg_dve, 1)
                    nc.vector.reciprocal(rdeg[:, :], rdeg[:, :]).then_inc(deg_dve, 1)
                    nc.vector.memset(tmp[:, :], 1.0).then_inc(deg_dve, 1)

                @block.scalar
                def _(act):
                    act.wait_ge(deg_dve, 2)
                    nc.scalar.activation(node_p[:, :], dinv[:, :], ACT.Sqrt).then_inc(root, 1)

                @block.tensor
                def _(pe):
                    def count(h, s):
                        pe.wait_ge(hot_ready, at(h, 1, 1))
                        for b in range(B):
                            last = nc.tensor.matmul(ps[:, 0, 0:T], hot_p[:, s, b, :], hot_t[:, s, b, :],
                                                    start=static(h) and h == 0 and b == 0, stop=False,
                                                    skip_group_check=True)
                        last.then_inc(hot_used, 1)

                    pairs(pe, 0, HALVES, count)
                    pe.wait_ge(hot_used, HALVES)
                    nc.tensor.matmul(ps[:, 0, 0:T], zeros[:, 0:P // 2].bitcast(F16), zeros[:, 0:T // 2].bitcast(F16),
                                     start=False, stop=True, skip_group_check=True).then_inc(deg_ready, 1)

        def phase_edges(k):
            width = widths[k]
            rels = {2: R16, 4: R8}.get(k, 0)
            types = {2: t16_f, 4: t8_f}.get(k)
            wrel = {2: w1t, 4: w3t}.get(k)
            q_n = rels // 2
            cut_at[0] = 0
            rows = cut([2, B, D if rels else width])
            dst_c = cut([2, B])
            same = cut([2, B, P])
            sums = cut([2, B, width])
            if k == 0:
                dup = cut([B, P])
                late = cut([B])
                shift = cut([B])
                hot8 = cut([B, R8])
            if rels:
                hot = cut([2, B, rels])
                wide = cut([2, rels, D])
                wide_t = cut([2, q_n, P])
                msg = cut([2, B, D])
            rhs = msg if rels else rows
            gathered = [sem(f"e{k}_gathered{s}") for s in range(2)]
            attrs = [sem(f"e{k}_attrs{s}") for s in range(2)] if k == 0 else None
            added = [sem(f"e{k}_added{q}") for q in range(2)]
            zeroed = sem(f"e{k}_zeroed")
            copied_in, copied_out = sem(f"e{k}_copied_in"), sem(f"e{k}_copied_out")
            cols_ok, dst_row, dst_same = sem(f"e{k}_cols_ok"), sem(f"e{k}_dst_row"), sem(f"e{k}_dst_same")
            chain, merged, evac = sem(f"e{k}_chain"), sem(f"e{k}_merged"), sem(f"e{k}_evac")
            if rels:
                spread, turned, turned_ok, typed, typed_ok = (
                    sem(f"e{k}_{n}") for n in ("spread", "turned", "turned_ok", "typed", "typed_ok"))
            K0 = 7
            per_bank = 3 if k == 0 else B
            sum_bank = 2 if k == 0 else 7
            dst_ps = ps[:, 0:2, :].rearrange("p a c -> p (a c)")[:, 0:B * P].rearrange("p (b c) -> p b c", b=B)

            def sum_ps(b):
                c = (b % per_bank) * width
                return ps[:, sum_bank + b // per_bank, c:c + width]

            def turned_ps(u):
                return ps[:, 2 + 2 * u:4 + 2 * u, :].rearrange("p a c -> p (a c)")[:, 0:q_n * P].rearrange(
                    "p (q c) -> p q c", q=q_n)

            with nc.Block() as block:
                @block.gpsimd
                def _(pool):
                    def body(h, s):
                        gather = not (static(h) and h >= HALVES)
                        scatter = not (static(h) and h < 2)
                        if gather:
                            if scatter:
                                reached(pool, spread if rels else merged, at(h, B, -B) if rels else at(h, 1, -1))
                                reached(pool, gathered[s], 16 * B * (h // 2) if static(h) else h[0] * (16 * B))
                            nc.gpsimd.tensor_copy(ixs[:, s, :], src_i[:, bass.ds(at(h, B, 0), B)]).then_inc(copied_in, 1)
                        if scatter:
                            reached(pool, evac, at(h, 1, -1))
                            nc.gpsimd.tensor_copy(ixo[:, s, :], out_i[:, bass.ds(at(h, B, -2 * B), B)]).then_inc(copied_out, 1)
                        if gather:
                            reached(pool, copied_in, at(h, 1, 1))
                        if scatter:
                            reached(pool, copied_out, at(h, 1, -1))
                        for b in range(B):
                            if gather:
                                nc.gpsimd.indirect_dma_start(
                                    out=rows[:, s, b, 0:D], out_offset=None, in_=table[k],
                                    in_offset=bass.IndirectOffsetOnAxis(ap=ixs[:, s, b:b + 1], axis=0)).then_inc(gathered[s], 16)
                            if scatter:
                                q = (s * B + b) % 2
                                if static(h):
                                    if (h - 2) * B + b >= 2:
                                        reached(pool, added[q], 16 * (((h - 2) * B + b) // 2))
                                else:
                                    reached(pool, added[q], h[0] * (16 * B) + 16 * ((s * B + b) // 2 - B))
                                nc.gpsimd.indirect_dma_start(
                                    out=agg[k][q], out_offset=bass.IndirectOffsetOnAxis(ap=ixo[:, s, b:b + 1], axis=0),
                                    in_=sums[:, s, b, :], in_offset=None, compute_op=ALU.add).then_inc(added[q], 16)

                    pairs(pool, 0, HALVES, body, tail=2)
                    for q in range(2):
                        reached(pool, added[q], 16 * (T // 2))

                @block.sync
                def _(sp):
                    if k + 1 < 5:
                        zero_aggregate(sp, k + 1, zeroed)
                    if k == 0:
                        ea = edge_attr[0:(P - 1) * T, :].rearrange("(p t) f -> p t f", t=T)
                        ea_last = edge_attr[(P - 1) * T:E, :].rearrange("(p t) f -> p t f", p=1)
                        mid = LAST // B // 2 * 2

                        def load_attr(h, s, last=None):
                            if not (static(h) and h < 2):
                                reached(sp, merged, at(h, 1, -1))
                            here = bass.ds(at(h, B, 0), B)
                            sp.dma_start(rows[0:112, s, :, D:2 * D], ea[0:112, here, :]).then_inc(attrs[s], 16)
                            sp.dma_start(rows[112:P - 1, s, :, D:2 * D], ea[112:P - 1, here, :]).then_inc(attrs[s], 16)
                            of, n = last or (here, B)
                            sp.dma_start(rows[P - 1:P, s, 0:n, D:2 * D], ea_last[:, of, :]).then_inc(attrs[s], 16)

                        pairs(sp, 0, mid, load_attr)
                        for h in range(mid, mid + 2):
                            n = max(min(LAST - h * B, B), 1)
                            load_attr(h, h % 2, (slice(LAST - n, LAST), n))
                        with sp.Fori(mid // 2 + 1, HALVES // 2, 1) as r:
                            for s in range(2):
                                load_attr((r, s), s, (slice(0, 1), 1))
                    if k + 1 < 5:
                        reached(sp, zeroed, 32)

                @block.tensor
                def _(pe):
                    def turn(h, s, b):
                        u = (s * B + b) % 2
                        reached(pe, spread, at(h, B, b + 1))
                        if not (static(h) and h * B + b < 2):
                            reached(pe, turned_ok, at(h, B, b - 1))
                        for q in range(q_n):
                            last = nc.tensor.transpose(
                                turned_ps(u)[:, q, :], wide[:, u, 2 * q:2 * q + 2, :].rearrange("p c f -> p (c f)"), ident[:, :])
                        last.then_inc(turned, 1)

                    def body(h, s):
                        reached(pe, cols_ok, at(h, 1, 1))
                        if not (static(h) and h < 1):
                            reached(pe, dst_same, at(h, 1, 0))
                        for b in range(B):
                            last = nc.tensor.transpose(dst_ps[:, b, :], dst_c[:, s, b:b + 1].to_broadcast([P, P]), ident[:, :])
                        last.then_inc(dst_row, 1)
                        if rels:
                            turn(h, s, 0)
                            for b in range(B):
                                u = (s * B + b) % 2
                                if b + 1 < B:
                                    turn(h, s, b + 1)
                                pe.wait_ge(turned_ok, at(h, B, b + 1))
                                if b == 0 and not (static(h) and h < 1):
                                    pe.wait_ge(typed_ok, at(h, 1, 0))
                                for q in range(q_n):
                                    last = nc.tensor.matmul(ps[:, 6, b * D:(b + 1) * D], wide_t[:, u, q, :], wrel[:, q, :],
                                                            start=q == 0, stop=q == q_n - 1)
                                last.then_inc(typed, 1)
                            pe.wait_ge(typed_ok, at(h, 1, 1))
                        else:
                            pe.wait_ge(gathered[s], 16 * B * (h // 2 + 1) if static(h) else h[0] * (16 * B) + 16 * B)
                        if k == 0:
                            pe.wait_ge(attrs[s], 48 * (h // 2 + 1) if static(h) else h[0] * 48 + 48)
                            pe.wait_ge(chain, at(h, K0, K0))
                        pe.wait_ge(dst_same, at(h, 1, 1))
                        if not (static(h) and h < 1):
                            pe.wait_ge(evac, at(h, 1, 0))
                        for b in range(B):
                            last = nc.tensor.matmul(sum_ps(b), same[:, s, b, :], rhs[:, s, b, :], start=True, stop=True)
                        last.then_inc(merged, 1)

                    pairs(pe, 0, HALVES, body)

                @block.vector
                def _(dve):
                    def body(h, s):
                        here = bass.ds(at(h, B, 0), B)
                        dve.wait_ge(dst_row, at(h, 1, 1))
                        if not (static(h) and h < 2):
                            dve.wait_ge(merged, at(h, 1, -1))
                        nc.vector.tensor_tensor(same[:, s, :, :], dst_ps, dst_c[:, s, :].unsqueeze(2).to_broadcast([P, B, P]),
                                                ALU.is_equal).then_inc(dst_same, 1)
                        if k == 0:
                            dve.wait_ge(dst_same, at(h, 1, 1))
                            nc.vector.tensor_tensor(dup, same[:, s, :, :], lower[:, :].unsqueeze(1).to_broadcast([P, B, P]),
                                                    ALU.mult).then_inc(chain, 1)
                            nc.vector.tensor_scalar(shift, dst_c[:, s, :], -1.0, trash_f[:, :], ALU.mult, ALU.add).then_inc(chain, 1)
                            nc.vector.tensor_tensor(hot8, t8_f[:, here].unsqueeze(2).to_broadcast([P, B, R8]),
                                                    iota16[:, 0:R8].unsqueeze(1).to_broadcast([P, B, R8]), ALU.is_equal).then_inc(chain, 1)
                            dve.wait_ge(chain, at(h, K0, 3))
                            nc.vector.tensor_reduce(late, dup, AX.X, ALU.max).then_inc(chain, 1)
                            nc.vector.tensor_tensor(rows[:, s, :, 2 * D:W0], hot8, w_f[:, here].unsqueeze(2).to_broadcast([P, B, R8]),
                                                    ALU.mult).then_inc(chain, 1)
                            dve.wait_ge(chain, at(h, K0, 5))
                            nc.vector.tensor_tensor(late, late, shift, ALU.mult).then_inc(chain, 1)
                            dve.wait_ge(chain, at(h, K0, 6))
                            nc.vector.tensor_tensor(out_i[:, here], late, dst_c[:, s, :], ALU.add).then_inc(chain, 1)
                            dve.wait_ge(chain, at(h, K0, 7))
                        if rels:
                            nc.vector.tensor_tensor(hot[:, s, :, :], types[:, here].unsqueeze(2).to_broadcast([P, B, rels]),
                                                    iota16[:, 0:rels].unsqueeze(1).to_broadcast([P, B, rels]), ALU.is_equal).then_inc(chain, 1)
                            kr = 1
                            if k == 4:
                                kr = 2
                                dve.wait_ge(chain, at(h, kr, 1))
                                nc.vector.tensor_tensor(hot[:, s, :, :], hot[:, s, :, :],
                                                        w_f[:, here].unsqueeze(2).to_broadcast([P, B, rels]), ALU.mult).then_inc(chain, 1)
                            dve.wait_ge(chain, at(h, kr, kr))
                            dve.wait_ge(gathered[s], 16 * B * (h // 2 + 1) if static(h) else h[0] * (16 * B) + 16 * B)
                            for b in range(B):
                                u = (s * B + b) % 2
                                if not (static(h) and h * B + b < 2):
                                    dve.wait_ge(turned, at(h, B, b - 1))
                                nc.vector.tensor_tensor(wide[:, u, :, :], rows[:, s, b, :].unsqueeze(1).to_broadcast([P, rels, D]),
                                                        hot[:, s, b, :].unsqueeze(2).to_broadcast([P, rels, D]), ALU.mult).then_inc(spread, 1)

                    pairs(dve, 0, HALVES, body)

                @block.scalar
                def _(act):
                    def body(h, s):
                        if not (static(h) and h < 2):
                            act.wait_ge(dst_same, at(h, 1, -1))
                            if k == 0:
                                act.wait_ge(chain, at(h, K0, -K0))
                        nc.scalar.copy(dst_c[:, s, :], dst_f[:, bass.ds(at(h, B, 0), B)]).then_inc(cols_ok, 1)
                        if rels:
                            for b in range(B):
                                u = (s * B + b) % 2
                                act.wait_ge(turned, at(h, B, b + 1))
                                if not (static(h) and h * B + b < 2):
                                    act.wait_ge(typed, at(h, B, b - 1))
                                nc.scalar.copy(wide_t[:, u, :, :], turned_ps(u)).then_inc(turned_ok, 1)
                            act.wait_ge(typed, at(h, B, B))
                            if not (static(h) and h < 2):
                                act.wait_ge(merged, at(h, 1, -1))
                            nc.scalar.copy(msg[:, s, :, :].rearrange("p b f -> p (b f)"), ps[:, 6, 0:B * D]).then_inc(typed_ok, 1)
                        act.wait_ge(merged, at(h, 1, 1))
                        if not (static(h) and h < 2):
                            for q in range(2):
                                if static(h):
                                    act.wait_ge(added[q], 16 * (((h - 1) * B + 1 - q) // 2))
                                else:
                                    act.wait_ge(added[q], h[0] * (16 * B) + 16 * (((s - 1) * B + 1 - q) // 2))
                        if k == 0:
                            full = B // per_bank
                            n = full * per_bank
                            nc.scalar.copy(sums[:, s, 0:n, :].rearrange("p (a b) w -> p a (b w)", a=full),
                                           ps[:, sum_bank:sum_bank + full, 0:per_bank * width])
                            nc.scalar.copy(sums[:, s, n:B, :].rearrange("p b w -> p (b w)"),
                                           ps[:, sum_bank + full, 0:(B - n) * width]).then_inc(evac, 1)
                        else:
                            nc.scalar.copy(sums[:, s, :, :].rearrange("p b w -> p (b w)"), ps[:, sum_bank, 0:B * width]).then_inc(evac, 1)

                    pairs(act, 0, HALVES, body)

        def nth(h, s, per, more=0):
            return per * (h // 2) + more if static(h) else h[0] * per + more

        def here4(h):
            return bass.ds(at(h, GN, 0), GN)

        def tile4(h, b):
            return at(h, GN, b)

        def layer_stats(h):
            for b in range(GN):
                one = bass.ds(tile4(h, b), 1)
                last = nc.vector.bn_stats(row_stats[:, one, :].rearrange("p a c -> p (a c)"),
                                          xr[:, one, :].rearrange("p a f -> p (a f)"))
            return last

        def store_rows(sp, to, done, tb, stored):
            def body(h, s):
                reached(sp, done, at(h, 1, 1))
                sp.dma_start(node_view(to)[:, here4(h), :], tb[:, s, :, :]).then_inc(stored[s], 16)
            return body

        def wait_stored(eng, stored, n=16):
            for s in range(2):
                eng.wait_ge(stored[s], n * (GROUPS // 2))

        def phase_norm_rows(k):
            cut_at[0] = 0
            add, diff, spread = (cut([T]) for _ in range(3))
            hn, tb = cut([2, GN, D]), cut([2, GN, D])
            step, root, normed, done = (sem(f"n{k}_{n}") for n in ("step", "root", "normed", "done"))
            stored = [sem(f"n{k}_stored{s}") for s in range(2)]
            with nc.Block() as block:
                @block.vector
                def _(dve):
                    m0, m1, v0, v1 = (row_stats[:, :, c] for c in (1, 4, 2, 5))
                    nc.vector.tensor_tensor(add, m0, m1, ALU.add).then_inc(step, 1)
                    nc.vector.tensor_tensor(diff, m0, m1, ALU.subtract).then_inc(step, 1)
                    nc.vector.tensor_tensor(spread, v0, v1, ALU.add).then_inc(step, 1)
                    dve.wait_ge(step, 3)
                    nc.vector.tensor_scalar(mean[:, :], add, 0.5, None, ALU.mult).then_inc(step, 1)
                    nc.vector.tensor_tensor(diff, diff, diff, ALU.mult).then_inc(step, 1)
                    dve.wait_ge(step, 5)
                    nc.vector.scalar_tensor_tensor(spread, diff, D / 4.0, spread, ALU.mult, ALU.add).then_inc(step, 1)
                    dve.wait_ge(step, 6)
                    nc.vector.tensor_scalar(spread, spread, 1.0 / D, EPS, ALU.mult, ALU.add).then_inc(step, 1)
                    dve.wait_ge(root, 1)
                    nc.vector.reciprocal(rstd[:, :], add).then_inc(step, 1)
                    dve.wait_ge(step, 8)
                    if k == 0:
                        nc.vector.tensor_tensor(rstd[:, :], rstd[:, :], dinv[:, :], ALU.mult).then_inc(step, 1)
                        dve.wait_ge(step, 9)

                    def body(h, s):
                        if not (static(h) and h < 2):
                            dve.wait_ge(done, at(h, 1, -1))
                        for b in range(GN):
                            one = bass.ds(tile4(h, b), 1)
                            last = nc.vector.tensor_scalar(hn[:, s, b, :], xr[:, one, :].rearrange("p a f -> p (a f)"),
                                                           mean[:, one], rstd[:, one], ALU.subtract, ALU.mult)
                        last.then_inc(normed, 1)

                    pairs(dve, 0, GROUPS, body)

                @block.scalar
                def _(act):
                    act.wait_ge(step, 7)
                    nc.scalar.activation(add, spread, ACT.Sqrt).then_inc(root, 1)

                    def body(h, s):
                        act.wait_ge(normed, at(h, 1, 1))
                        if not (static(h) and h < 2):
                            act.wait_ge(stored[s], nth(h, s, 16))
                        nc.scalar.activation(tb[:, s, :, :], hn[:, s, :, :], ACT.Relu).then_inc(done, 1)

                    pairs(act, 0, GROUPS, body)

                @block.sync
                def _(sp):
                    pairs(sp, 0, GROUPS, store_rows(sp, table[k], done, tb, stored))
                    wait_stored(sp, stored)

        def phase_gcn(k):
            wgt = (w01, w02)[k]
            cut_at[0] = 0
            la, lb, lt, u, v, z = (cut([2, GN, D]) for _ in range(6))
            ra, rb, rd = (cut([2, GN, R8]) for _ in range(3))
            zt = cut([2, COLS])[0:D + 1]
            tb = cut([2, GN, D])
            loaded = [sem(f"g{k}_loaded{s}") for s in range(2)]
            stored = [sem(f"g{k}_stored{s}") for s in range(2)]
            deg_stored = [sem(f"g{k}_deg_stored{s}") for s in range(2)]
            ones, added, z_chain, z_t, zt_ok, y_ok, y_used, done, deg_sum = (
                sem(f"g{k}_{n}") for n in ("ones", "added", "z_chain", "z_t", "zt_ok", "y_ok", "y_used", "done", "deg_sum"))
            n_loads = 5 if k == 0 else 3

            with nc.Block() as block:
                @block.sync
                def _(sp):
                    store = store_rows(sp, table[k + 1], done, tb, stored)

                    def body(h, s):
                        if not (static(h) and h >= GROUPS):
                            if not (static(h) and h < 2):
                                reached(sp, added, at(h, 1, -1))
                                reached(sp, z_chain, at(h, 2, -3))
                            for to, of in ((la, agg[k][0]), (lb, agg[k][1]), (lt, table[k])):
                                sp.dma_start(to[:, s, :, :], node_view(of[0:ROWS, 0:D])[:, here4(h), :]).then_inc(loaded[s], 16)
                            if k == 0:
                                for to, of in ((ra, agg[0][0]), (rb, agg[0][1])):
                                    sp.dma_start(to[:, s, :, :], node_view(of[0:ROWS, 2 * D:W0])[:, here4(h), :]).then_inc(loaded[s], 16)
                        if k == 0 and not (static(h) and h < 2):
                            g = (h - 2) if static(h) else (h[0] - 1, s)
                            reached(sp, deg_sum, at(g, 1, 1))
                            sp.dma_start(node_view(rel_deg[0:ROWS, :])[:, here4(g), :], rd[:, s, :, :]).then_inc(deg_stored[s], 16)
                            store(g, s)

                    pairs(sp, 0, GROUPS, body, tail=2 if k == 0 else 0)
                    if k == 0:
                        wait_stored(sp, stored)
                        wait_stored(sp, deg_stored)

                @block.gpsimd
                def _(pool):
                    nc.gpsimd.memset(zt[D:D + 1, :, :], 1.0).then_inc(ones, 1)
                    pool.wait_ge(ones, 1)

                    def body(h, s):
                        reached(pool, loaded[s], nth(h, s, 16 * n_loads, 16 * n_loads))
                        if not (static(h) and h < 2):
                            reached(pool, z_chain, at(h, 2, -3))
                        if k == 0:
                            if not (static(h) and h < 2):
                                reached(pool, deg_stored[s], nth(h, s, 16))
                            nc.gpsimd.tensor_tensor(rd[:, s, :, :], ra[:, s, :, :], rb[:, s, :, :], ALU.add).then_inc(deg_sum, 1)
                        nc.gpsimd.tensor_tensor(u[:, s, :, :], lb[:, s, :, :], lt[:, s, :, :], ALU.add).then_inc(added, 1)

                    pairs(pool, 0, GROUPS, body)

                @block.vector
                def _(dve):
                    def sum_up(h, s):
                        dve.wait_ge(added, at(h, 1, 1))
                        dve.wait_ge(loaded[s], nth(h, s, 16 * n_loads, 16 * n_loads))
                        nc.vector.tensor_tensor(v[:, s, :, :], la[:, s, :, :], u[:, s, :, :], ALU.add).then_inc(z_chain, 1)
                        dve.wait_ge(z_chain, at(h, 2, 1))
                        if not (static(h) and h < 2):
                            dve.wait_ge(z_t, at(h, 1, -1))
                        nc.vector.tensor_tensor(z[:, s, :, :], v[:, s, :, :],
                                                dinv[:, here4(h)].unsqueeze(2).to_broadcast([P, GN, D]), ALU.mult).then_inc(z_chain, 1)

                    def finish(h, s):
                        dve.wait_ge(y_ok, at(h, 1, 1))
                        here = xr[:, here4(h), :]
                        nc.vector.scalar_tensor_tensor(here, ps[:, 2 + s, 0:GN * D].rearrange("p (b f) -> p b f", b=GN), 0.0,
                                                       here, ALU.max, ALU.add).then_inc(y_used, 1)
                        dve.wait_ge(y_used, at(h, 1, 1))
                        layer_stats(h)

                    def body(h, s):
                        if not (static(h) and h >= GROUPS):
                            sum_up(h, s)
                        if not (static(h) and h < 2):
                            finish((h - 2) if static(h) else (h[0] - 1, s), s)

                    if k == 0:
                        pairs(dve, 0, GROUPS, sum_up)
                    else:
                        pairs(dve, 0, GROUPS, body, tail=2)

                @block.tensor
                def _(pe):
                    def turn(h, s):
                        reached(pe, z_chain, at(h, 2, 2))
                        if not (static(h) and h < 2):
                            reached(pe, zt_ok, at(h, 1, -1))
                        for b in range(GN):
                            last = nc.tensor.transpose(ps[0:D, s, b * P:(b + 1) * P], z[:, s, b, :], ident[:, :])
                        last.then_inc(z_t, 1)

                    def multiply(h, s):
                        pe.wait_ge(zt_ok, at(h, 1, 1))
                        if not (static(h) and h < 2):
                            pe.wait_ge(y_used if k else done, at(h, 1, -1))
                        for b in range(GN):
                            last = nc.tensor.matmul(ps[:, 2 + s, b * D:(b + 1) * D], zt[:, s, b * P:(b + 1) * P], wgt[:, :],
                                                    start=True, stop=True)
                        last.then_inc(y_ok, 1)

                    pe.wait_ge(ones, 1)
                    lagged(pe, turn, multiply, 1)

                @block.scalar
                def _(act):
                    def copy(h, s):
                        act.wait_ge(z_t, at(h, 1, 1))
                        if not (static(h) and h < 2):
                            act.wait_ge(y_ok, at(h, 1, -1))
                        nc.scalar.copy(zt[0:D, s, :], ps[0:D, s, :]).then_inc(zt_ok, 1)

                    def rows0(h, s):
                        act.wait_ge(y_ok, at(h, 1, 1))
                        if not (static(h) and h < 2):
                            act.wait_ge(stored[s], nth(h, s, 16))
                        for b in range(GN):
                            last = nc.scalar.activation(tb[:, s, b, :], ps[:, 2 + s, b * D:(b + 1) * D], ACT.Relu,
                                                        scale=dinv[:, bass.ds(tile4(h, b), 1)])
                        last.then_inc(done, 1)

                    if k == 0:
                        lagged(act, copy, rows0, 2)
                    else:
                        pairs(act, 0, GROUPS, copy)

        def lagged(eng, early, late, lag):
            def body(h, s):
                if not (static(h) and h >= GROUPS):
                    early(h, s)
                if static(h):
                    if h >= lag:
                        late(h - lag, (h - lag) % 2)
                else:
                    r = h[0]
                    g = {0: (r, s), 2: (r - 1, s), 1: ((r - 1, 1) if s == 0 else (r, 0))}[lag]
                    late(g, g[1])

            pairs(eng, 0, GROUPS, body, tail=lag)

        def phase_add_rows():
            k = 2
            cut_at[0] = 0
            la, lb, u = (cut([2, GN, D]) for _ in range(3))
            loaded = [sem(f"a_loaded{s}") for s in range(2)]
            added, x_ok = sem("a_added"), sem("a_x_ok")
            with nc.Block() as block:
                @block.sync
                def _(sp):
                    def load(h, s):
                        if not (static(h) and h < 2):
                            reached(sp, added, at(h, 1, -1))
                        for to, of in ((la, agg[k][0]), (lb, agg[k][1])):
                            sp.dma_start(to[:, s, :, :], node_view(of[0:ROWS, :])[:, here4(h), :]).then_inc(loaded[s], 16)

                    pairs(sp, 0, GROUPS, load)

                @block.gpsimd
                def _(pool):
                    def body(h, s):
                        reached(pool, loaded[s], nth(h, s, 32, 32))
                        if not (static(h) and h < 2):
                            reached(pool, x_ok, at(h, 1, -1))
                        nc.gpsimd.tensor_tensor(u[:, s, :, :], la[:, s, :, :], lb[:, s, :, :], ALU.add).then_inc(added, 1)

                    pairs(pool, 0, GROUPS, body)

                @block.vector
                def _(dve):
                    def body(h, s):
                        dve.wait_ge(added, at(h, 1, 1))
                        here = xr[:, here4(h), :]
                        nc.vector.tensor_tensor(here, here, u[:, s, :, :], ALU.add).then_inc(x_ok, 1)
                        dve.wait_ge(x_ok, at(h, 1, 1))
                        layer_stats(h)

                    pairs(dve, 0, GROUPS, body)

        def stats_loops(dve, lag, body, early=None):
            def step(valid):
                def run(h, s):
                    if early and not (static(h) and h >= GROUPS):
                        early(h, s)
                    if static(h):
                        if h >= lag:
                            body(h - lag, s, COLS if h - lag < FULL else COLS - GN)
                    else:
                        body((h[0] - lag // 2, s), s, valid)
                return run

            assert FULL % 2 == 0 and lag % 2 == 0
            pairs(dve, 0, FULL + lag, step(COLS), peel=2 + lag)
            with dve.Fori((FULL + lag) // 2, GROUPS // 2, 1) as r:
                for s in range(2):
                    step(COLS - GN)((r, s), s)
            for h in range(GROUPS, GROUPS + lag):
                step(COLS - GN)(h, h % 2)

        def edge_degrees(pool, first, end, gathered, copied, used):
            def body(h, s):
                later = not (static(h) and h < first + 2)
                if later:
                    n = nth(h, s, 16 * B, -16 * B * (first // 2))
                    reached(pool, gathered[s], n)
                    nc.gpsimd.tensor_copy(edge_rel[:, bass.ds(at(h, B, -2 * B), B), :], rel_rows[:, s, :, :]).then_inc(used, 1)
                    reached(pool, used, at(h, 1, -1 - first))
                if not (static(h) and h >= end):
                    nc.gpsimd.tensor_copy(ixs[:, s, :], dst_i[:, bass.ds(at(h, B, 0), B)]).then_inc(copied, 1)
                    reached(pool, copied, at(h, 1, 1 - first))
                    for b in range(B):
                        nc.gpsimd.indirect_dma_start(
                            out=rel_rows[:, s, b, :], out_offset=None, in_=rel_deg,
                            in_offset=bass.IndirectOffsetOnAxis(ap=ixs[:, s, b:b + 1], axis=0)).then_inc(gathered[s], 16)

            pairs(pool, first, end, body, tail=2)

        rel_rows = sb("rel_rows", [P, 2, B, R8])

        def phase_mean():
            k = 3
            cut_at[0] = 0
            la, lb, lc, ld, lt, u, v, w1_, w2_, g = (cut([2, GN, D]) for _ in range(10))
            gt = cut([2, COLS])[0:D + 1]
            loaded = [sem(f"m_loaded{s}") for s in range(2)]
            stored = [sem(f"m_stored{s}") for s in range(2)]
            one = sb("eps_plus_one", [P, 1])
            one_ok = sem("m_one_ok")
            ones, added, chain, g_t, gt_ok, y_ok, y_used = (
                sem(f"m_{n}") for n in ("ones", "added", "chain", "g_t", "gt_ok", "y_ok", "y_used"))
            gd = g_dram.rearrange("f (g c) -> f g c", c=COLS)
            with nc.Block() as block:
                @block.sync
                def _(sp):
                    def load(h, s):
                        if not (static(h) and h < 2):
                            reached(sp, added, at(h, 1, -1))
                            reached(sp, chain, at(h, 3, -3))
                        for to, of in ((la, agg[k][0]), (lb, agg[k][1]), (lt, table[k])):
                            sp.dma_start(to[:, s, :, :], node_view(of[0:ROWS, 0:D])[:, here4(h), :]).then_inc(loaded[s], 16)
                        for to, of in ((lc, agg[0][0]), (ld, agg[0][1])):
                            sp.dma_start(to[:, s, :, :], node_view(of[0:ROWS, D:2 * D])[:, here4(h), :]).then_inc(loaded[s], 16)

                    def store(h, s):
                        reached(sp, gt_ok, at(h, 1, 1))
                        sp.dma_start(gd[:, bass.ds(at(h, 1, 0), 1), :].rearrange("f a c -> f (a c)"), gt[0:D, s, :]).then_inc(stored[s], 16)

                    lagged(sp, load, store, 2)
                    wait_stored(sp, stored)

                @block.gpsimd
                def _(pool):
                    nc.gpsimd.memset(gt[D:D + 1, :, :], 1.0).then_inc(ones, 1)
                    pool.wait_ge(ones, 1)

                    def body(h, s):
                        reached(pool, loaded[s], nth(h, s, 80, 80))
                        if not (static(h) and h < 2):
                            reached(pool, chain, at(h, 3, -3))
                        nc.gpsimd.tensor_tensor(u[:, s, :, :], la[:, s, :, :], lb[:, s, :, :], ALU.add)
                        nc.gpsimd.tensor_tensor(v[:, s, :, :], lc[:, s, :, :], ld[:, s, :, :], ALU.add).then_inc(added, 1)

                    pairs(pool, 0, GROUPS, body)

                @block.vector
                def _(dve):
                    nc.vector.tensor_scalar(one[:, :], eps1[:, :], 1.0, None, ALU.add).then_inc(one_ok, 1)
                    dve.wait_ge(one_ok, 1)

                    def mean(h, s):
                        dve.wait_ge(added, at(h, 1, 1))
                        nc.vector.tensor_tensor(w1_[:, s, :, :], u[:, s, :, :], v[:, s, :, :], ALU.add).then_inc(chain, 1)
                        dve.wait_ge(chain, at(h, 3, 1))
                        nc.vector.tensor_tensor(w2_[:, s, :, :], w1_[:, s, :, :],
                                                rdeg[:, here4(h)].unsqueeze(2).to_broadcast([P, GN, D]), ALU.mult).then_inc(chain, 1)
                        dve.wait_ge(chain, at(h, 3, 2))
                        dve.wait_ge(loaded[s], nth(h, s, 80, 80))
                        if not (static(h) and h < 2):
                            dve.wait_ge(g_t, at(h, 1, -1))
                        nc.vector.scalar_tensor_tensor(g[:, s, :, :], lt[:, s, :, :], one[:, :], w2_[:, s, :, :],
                                                       ALU.mult, ALU.add).then_inc(chain, 1)

                    def stat(h, s, valid):
                        dve.wait_ge(y_ok, at(h, 1, 1))
                        nc.vector.bn_stats(bnst[:, bass.ds(at(h, 1, 0), 1), :].rearrange("p a c -> p (a c)"),
                                           ps[:, 2 + s, 0:valid]).then_inc(y_used, 1)

                    stats_loops(dve, 2, stat, mean)

                @block.tensor
                def _(pe):
                    def turn(h, s):
                        reached(pe, chain, at(h, 3, 3))
                        if not (static(h) and h < 2):
                            reached(pe, gt_ok, at(h, 1, -1))
                        for b in range(GN):
                            last = nc.tensor.transpose(ps[0:D, s, b * P:(b + 1) * P], g[:, s, b, :], ident[:, :])
                        last.then_inc(g_t, 1)

                    def multiply(h, s):
                        pe.wait_ge(gt_ok, at(h, 1, 1))
                        if not (static(h) and h < 2):
                            pe.wait_ge(y_used, at(h, 1, -1))
                        nc.tensor.matmul(ps[:, 2 + s, :], w21[:, :], gt[:, s, :], start=True, stop=True).then_inc(y_ok, 1)

                    pe.wait_ge(ones, 1)
                    lagged(pe, turn, multiply, 1)

                @block.scalar
                def _(act):
                    def copy(h, s):
                        act.wait_ge(g_t, at(h, 1, 1))
                        if not (static(h) and h < 2):
                            act.wait_ge(y_ok, at(h, 1, -1))
                            act.wait_ge(stored[s], nth(h, s, 16))
                        nc.scalar.copy(gt[0:D, s, :].rearrange("f (p b) -> f b p", b=GN),
                                       ps[0:D, s, :].rearrange("f (b p) -> f b p", b=GN)).then_inc(gt_ok, 1)

                    pairs(act, 0, GROUPS, copy)

        def norm_factors(dve, nrm, n, gamma, beta, step, root):
            nc.vector.bn_aggr(nrm[:, 0:2], bnst[0:n, :, :].rearrange("p g c -> p (g c)")).then_inc(step, 1)
            dve.wait_ge(step, 1)
            nc.vector.tensor_scalar(nrm[:, 4:5], nrm[:, 1:2], EPS, None, ALU.add).then_inc(step, 1)
            dve.wait_ge(root, 1)
            nc.vector.reciprocal(nrm[:, 4:5], nrm[:, 6:7]).then_inc(step, 1)
            dve.wait_ge(step, 3)
            nc.vector.tensor_tensor(nrm[:, 2:3], nrm[:, 4:5], gamma, ALU.mult).then_inc(step, 1)
            dve.wait_ge(step, 4)
            nc.vector.tensor_tensor(nrm[:, 5:6], nrm[:, 0:1], nrm[:, 2:3], ALU.mult).then_inc(step, 1)
            dve.wait_ge(step, 5)
            nc.vector.tensor_tensor(nrm[:, 3:4], beta, nrm[:, 5:6], ALU.subtract).then_inc(step, 1)

        def norm_root(act, nrm, step, root):
            act.wait_ge(step, 2)
            nc.scalar.activation(nrm[:, 6:7], nrm[:, 4:5], ACT.Sqrt).then_inc(root, 1)
            act.wait_ge(step, 6)

        SPLIT = HALVES // 4 * 2

        def phase_hidden():
            cut_at[0] = 0
            gt = cut([2, COLS])[0:D + 1]
            a = cut([2, COLS])
            y = cut([2, COLS])[0:D]
            loaded = [sem(f"h_loaded{s}") for s in range(2)]
            stored = [sem(f"h_stored{s}") for s in range(2)]
            rel_got = [sem(f"h_rel_got{s}") for s in range(2)]
            root = sem("h_root")
            step, ones, u_ok, a_ok, v_ok, y_ok, y_used, copied, rel_used = (
                sem(f"h_{n}") for n in ("step", "ones", "u_ok", "a_ok", "v_ok", "y_ok", "y_used", "copied", "rel_used"))
            gd = g_dram.rearrange("f (g c) -> f g c", c=COLS)
            yd = y_dram.rearrange("f (g c) -> f g c", c=COLS)
            with nc.Block() as block:
                @block.gpsimd
                def _(pool):
                    nc.gpsimd.memset(gt[D:D + 1, :, :], 1.0).then_inc(ones, 1)
                    pool.wait_ge(ones, 1)
                    edge_degrees(pool, 0, SPLIT, rel_got, copied, rel_used)

                @block.sync
                def _(sp):
                    def load(h, s):
                        if not (static(h) and h < 2):
                            reached(sp, u_ok, at(h, 1, -1))
                        sp.dma_start(gt[0:D, s, :], gd[:, bass.ds(at(h, 1, 0), 1), :].rearrange("f a c -> f (a c)")).then_inc(loaded[s], 16)

                    def store(h, s):
                        reached(sp, y_ok, at(h, 1, 1))
                        sp.dma_start(yd[:, bass.ds(at(h, 1, 0), 1), :].rearrange("f a c -> f (a c)"), y[:, s, :]).then_inc(stored[s], 16)

                    lagged(sp, load, store, 2)
                    wait_stored(sp, stored)

                @block.vector
                def _(dve):
                    norm_factors(dve, nrm1, P, gb1[:, 0:1], gb1[:, 1:2], step, root)

                    def stat(h, s, valid):
                        dve.wait_ge(y_ok, at(h, 1, 1))
                        nc.vector.bn_stats(bnst[0:D, bass.ds(at(h, 1, 0), 1), :].rearrange("p a c -> p (a c)"),
                                           y[:, s, 0:valid]).then_inc(y_used, 1)

                    stats_loops(dve, 0, stat)

                @block.tensor
                def _(pe):
                    def first(h, s):
                        pe.wait_ge(loaded[s], nth(h, s, 16, 16))
                        if not (static(h) and h < 2):
                            pe.wait_ge(a_ok, at(h, 1, -1))
                        nc.tensor.matmul(ps[:, s, :], w21[:, :], gt[:, s, :], start=True, stop=True).then_inc(u_ok, 1)

                    def second(h, s):
                        pe.wait_ge(a_ok, at(h, 1, 1))
                        if not (static(h) and h < 2):
                            pe.wait_ge(y_ok, at(h, 1, -1))
                        nc.tensor.matmul(ps[0:D, 2 + s, :], w22[:, :], a[:, s, :], start=True, stop=True).then_inc(v_ok, 1)

                    pe.wait_ge(ones, 1)
                    lagged(pe, first, second, 1)

                @block.scalar
                def _(act):
                    def hidden(h, s):
                        act.wait_ge(u_ok, at(h, 1, 1))
                        if not (static(h) and h < 2):
                            act.wait_ge(v_ok, at(h, 1, -1))
                        nc.scalar.activation(a[:, s, :], ps[:, s, :], ACT.Relu, bias=nrm1[:, 3:4], scale=nrm1[:, 2:3]).then_inc(a_ok, 1)

                    def result(h, s):
                        act.wait_ge(v_ok, at(h, 1, 1))
                        if not (static(h) and h < 2):
                            act.wait_ge(stored[s], nth(h, s, 16))
                            act.wait_ge(y_used, at(h, 1, -1))
                        nc.scalar.activation(y[:, s, :], ps[0:D, 2 + s, :], ACT.Identity, bias=gb2[:, 2:3]).then_inc(y_ok, 1)

                    norm_root(act, nrm1, step, root)
                    lagged(act, hidden, result, 1)

        def phase_second_norm():
            cut_at[0] = 0
            y = cut([2, COLS])[0:D]
            r_ = cut([2, COLS])[0:D]
            loaded = [sem(f"s_loaded{s}") for s in range(2)]
            rel_got = [sem(f"s_rel_got{s}") for s in range(2)]
            step, root, r_ok, r_t, x_ok, copied, rel_used = (
                sem(f"s_{n}") for n in ("step", "root", "r_ok", "r_t", "x_ok", "copied", "rel_used"))
            yd = y_dram.rearrange("f (g c) -> f g c", c=COLS)
            with nc.Block() as block:
                @block.gpsimd
                def _(pool):
                    edge_degrees(pool, SPLIT, HALVES, rel_got, copied, rel_used)

                @block.sync
                def _(sp):
                    def load(h, s):
                        if not (static(h) and h < 2):
                            reached(sp, r_ok, at(h, 1, -1))
                        sp.dma_start(y[:, s, :], yd[:, bass.ds(at(h, 1, 0), 1), :].rearrange("f a c -> f (a c)")).then_inc(loaded[s], 16)

                    pairs(sp, 0, GROUPS, load)

                @block.tensor
                def _(pe):
                    def turn(h, s):
                        reached(pe, r_ok, at(h, 1, 1))
                        if not (static(h) and h < 2):
                            reached(pe, x_ok, at(h, 1, -1))
                        for b in range(GN):
                            last = nc.tensor.transpose(ps[:, s, b * D:(b + 1) * D],
                                                       r_[:, s, :].rearrange("f (p b) -> f b p", b=GN)[:, b, :], ident[0:D, 0:D])
                        last.then_inc(r_t, 1)

                    pairs(pe, 0, GROUPS, turn)

                @block.vector
                def _(dve):
                    norm_factors(dve, nrm2, D, gb2[:, 0:1], gb2[:, 1:2], step, root)

                    def body(h, s):
                        dve.wait_ge(r_t, at(h, 1, 1))
                        here = xr[:, here4(h), :]
                        nc.vector.tensor_tensor(here, here, ps[:, s, 0:GN * D].rearrange("p (b f) -> p b f", b=GN), ALU.add).then_inc(x_ok, 1)
                        dve.wait_ge(x_ok, at(h, 1, 1))
                        layer_stats(h)

                    pairs(dve, 0, GROUPS, body)

                @block.scalar
                def _(act):
                    def relu(h, s):
                        act.wait_ge(loaded[s], nth(h, s, 16, 16))
                        if not (static(h) and h < 2):
                            act.wait_ge(r_t, at(h, 1, -1))
                        nc.scalar.activation(r_[:, s, :], y[:, s, :], ACT.Relu, bias=nrm2[:, 3:4], scale=nrm2[:, 2:3]).then_inc(r_ok, 1)

                    norm_root(act, nrm2, step, root)
                    pairs(act, 0, GROUPS, relu)

        def phase_edge_weights():
            step = sem("w_step")
            with nc.Block() as block:
                @block.vector
                def _(dve):
                    cut_at[0] = 0
                    hot = cut([T, R8])
                    own = cut([T])
                    nc.vector.tensor_tensor(hot, t8_f[:, :].unsqueeze(2).to_broadcast([P, T, R8]),
                                            iota16[:, 0:R8].unsqueeze(1).to_broadcast([P, T, R8]), ALU.is_equal).then_inc(step, 1)
                    dve.wait_ge(step, 1)
                    nc.vector.tensor_tensor(hot, hot, edge_rel[:, :, :], ALU.mult).then_inc(step, 1)
                    dve.wait_ge(step, 2)
                    nc.vector.tensor_reduce(own, hot, AX.X, ALU.add).then_inc(step, 1)
                    dve.wait_ge(step, 3)
                    nc.vector.reciprocal(own, own).then_inc(step, 1)
                    dve.wait_ge(step, 4)
                    nc.vector.tensor_tensor(w_f[:, :], w_f[:, :], own, ALU.mult).then_inc(step, 1)

        def phase_last():
            k = 4
            cut_at[0] = 0
            la, lb, lt, u, v, o = (cut([2, GN, D]) for _ in range(6))
            ht = cut([2, COLS])[0:D + 2]
            loaded = [sem(f"l_loaded{s}") for s in range(2)]
            stored = [sem(f"l_stored{s}") for s in range(2)]
            ones, added, h_t, ht_ok, y_ok, v_chain = (sem(f"l_{n}") for n in ("ones", "added", "h_t", "ht_ok", "y_ok", "v_chain"))
            ov = out[0:(P - 1) * T, :].rearrange("(p t) f -> p t f", t=T)
            ov_last = out[(P - 1) * T:N, :].rearrange("(p t) f -> p t f", p=1)
            with nc.Block() as block:
                @block.sync
                def _(sp):
                    def load(h, s):
                        if not (static(h) and h < 2):
                            reached(sp, added, at(h, 1, -1))
                            reached(sp, h_t, at(h, 1, -1))
                        for to, of in ((la, agg[k][0]), (lb, agg[k][1]), (lt, table[k])):
                            sp.dma_start(to[:, s, :, :], node_view(of[0:ROWS, :])[:, here4(h), :]).then_inc(loaded[s], 16)

                    pairs(sp, 0, GROUPS, load)

                @block.gpsimd
                def _(pool):
                    nc.gpsimd.memset(ht[D:D + 2, :, :], 1.0).then_inc(ones, 1)
                    pool.wait_ge(ones, 1)

                    def body(h, s):
                        reached(pool, loaded[s], nth(h, s, 48, 48))
                        if not (static(h) and h < 2):
                            reached(pool, v_chain, at(h, 2, -3))
                        nc.gpsimd.tensor_tensor(u[:, s, :, :], la[:, s, :, :], lb[:, s, :, :], ALU.add).then_inc(added, 1)

                    pairs(pool, 0, GROUPS, body)

                @block.tensor
                def _(pe):
                    def turn(h, s):
                        reached(pe, loaded[s], nth(h, s, 48, 48))
                        if not (static(h) and h < 2):
                            reached(pe, ht_ok, at(h, 1, -1))
                        for b in range(GN):
                            last = nc.tensor.transpose(ps[0:D, s, b * P:(b + 1) * P], lt[:, s, b, :], ident[:, :])
                        last.then_inc(h_t, 1)

                    def multiply(h, s):
                        pe.wait_ge(ht_ok, at(h, 1, 1))
                        if not (static(h) and h < 2):
                            pe.wait_ge(v_chain, at(h, 2, -3))
                        for b in range(GN):
                            last = nc.tensor.matmul(ps[:, 2 + s, b * D:(b + 1) * D], ht[:, s, b * P:(b + 1) * P], w3s[:, :],
                                                    start=True, stop=True)
                        last.then_inc(y_ok, 1)

                    pe.wait_ge(ones, 1)
                    lagged(pe, turn, multiply, 1)

                @block.vector
                def _(dve):
                    def body(h, s):
                        dve.wait_ge(added, at(h, 1, 1))
                        dve.wait_ge(y_ok, at(h, 1, 1))
                        nc.vector.tensor_tensor(v[:, s, :, :], ps[:, 2 + s, 0:GN * D].rearrange("p (b f) -> p b f", b=GN),
                                                u[:, s, :, :], ALU.add).then_inc(v_chain, 1)
                        dve.wait_ge(v_chain, at(h, 2, 1))
                        if not (static(h) and h < 2):
                            n = nth(h, s, 48) if not static(h) else 48 * (h // 2)
                            dve.wait_ge(stored[s], n)
                        nc.vector.scalar_tensor_tensor(o[:, s, :, :], v[:, s, :, :], 0.0, xr[:, here4(h), :],
                                                       ALU.max, ALU.add).then_inc(v_chain, 1)

                    pairs(dve, 0, GROUPS, body)

                @block.scalar
                def _(act):
                    def copy(h, s):
                        act.wait_ge(h_t, at(h, 1, 1))
                        if not (static(h) and h < 2):
                            act.wait_ge(y_ok, at(h, 1, -1))
                        nc.scalar.copy(ht[0:D, s, :], ps[0:D, s, :]).then_inc(ht_ok, 1)

                    def store(real):
                        def run(h, s):
                            reached(act, v_chain, at(h, 2, 2))
                            act.dma_start(ov[0:112, here4(h), :], o[0:112, s, :, :]).then_inc(stored[s], 16)
                            act.dma_start(ov[112:P - 1, here4(h), :], o[112:P - 1, s, :, :]).then_inc(stored[s], 16)
                            if real:
                                act.dma_start(ov_last[:, here4(h), :], o[P - 1:P, s, :, :]).then_inc(stored[s], 16)
                            else:
                                act.sem_inc(stored[s], 16)
                        return run

                    def step(real):
                        def run(h, s):
                            if not (static(h) and h >= GROUPS):
                                copy(h, s)
                            if static(h):
                                if h >= 2:
                                    store(h - 2 < FULL)(h - 2, s)
                            else:
                                store(real)((h[0] - 1, s), s)
                        return run

                    pairs(act, 0, FULL + 2, step(True), peel=4)
                    with act.Fori((FULL + 2) // 2, GROUPS // 2, 1) as r:
                        for s in range(2):
                            step(False)((r, s), s)
                    for h in range(GROUPS, GROUPS + 2):
                        step(False)(h, h % 2)
                    wait_stored(act, stored, 48)

        phase(phase_plan)
        phase(phase_norm_rows, 0)
        phase(phase_edges, 0)
        phase(phase_gcn, 0)
        phase(phase_edges, 1)
        phase(phase_gcn, 1)
        phase(phase_norm_rows, 2)
        phase(phase_edges, 2)
        phase(phase_add_rows)
        phase(phase_norm_rows, 3)
        phase(phase_edges, 3)
        phase(phase_mean)
        phase(phase_hidden)
        phase(phase_second_norm)
        phase(phase_norm_rows, 4)
        phase(phase_edge_weights)
        phase(phase_edges, 4)
        phase(phase_last)


_INS = ["x", "src", "dst", "edge_attr_64", "edge_type_16", "edge_type_8", "edge_weight", "L0_gnn_W1", "L0_gnn_b1",
        "L0_gnn_W2", "L0_gnn_b2", "L1_gnn_weight", "L2_gnn_eps", "L2_gnn_W1", "L2_gnn_b1", "L2_gnn_gamma1",
        "L2_gnn_beta1", "L2_gnn_W2", "L2_gnn_b2", "L2_gnn_gamma2", "L2_gnn_beta2", "L3_gnn_W_linear",
        "L3_gnn_b_linear", "L3_gnn_W_self", "L3_gnn_b_self"]


def kernel(**inputs):
    import numpy as np
    import concourse.bacc as bacc
    from concourse.bass_utils import run_bass_kernel_spmd

    nc = bacc.Bacc("TRN2", target_bir_lowering=False, num_devices=1)
    arrays, args = {}, []
    for name in _INS:
        a = np.ascontiguousarray(inputs[name])
        arrays[f"in_{name}"] = a
        args.append(nc.dram_tensor(f"in_{name}", a.shape, mybir.dt.from_np(a.dtype), kind="ExternalInput").ap())
    out = nc.dram_tensor("out", (N, D), F32, kind="ExternalOutput").ap()
    build(nc, *args, out)
    r = run_bass_kernel_spmd(nc, [arrays], core_ids=[0])
    return r.results[0]["out"]
```
